# Optimizing a Trainium2 kernel written in Bass

```python
import numpy as np
import jax
import jax.numpy as jnp

def _softmax(x, axis=-1):
    return jax.nn.softmax(x, axis=axis)

def _gelu(x):
    return jax.nn.gelu(x, approximate=True)

def _silu(x):
    return jax.nn.silu(x)

def _sigmoid(x):
    return jax.nn.sigmoid(x)

def _layernorm(x, axis=-1, eps=1e-05):
    m = jnp.mean(x, axis=axis, keepdims=True)
    v = jnp.var(x, axis=axis, keepdims=True)
    return (x - m) / jnp.sqrt(v + eps)

def _scatter_add(tgt, idx, src, axis=0):
    return tgt.at[idx].add(src)

def _segment_sum(src, seg, n):
    return jax.ops.segment_sum(src, seg, n)
kernel_name = 'mk_dlrm_tower_d1_rec_r8_6ca9dd'

def setup_inputs(seed: int=0):
    np.random.seed(seed)
    _w = jnp.asarray

    def _rec_inputs():
        import jax
        import jax.numpy as jnp
        _tk = jax.random.key(seed)
        ids = jnp.stack([jax.random.randint(jax.random.fold_in(_tk, 200 + f), (512,), 0, v, jnp.int32) for f, v in enumerate([1000, 1250, 125000, 1000, 1250, 1250, 1250, 1250, 1250, 1250, 1250, 12500, 1250, 1250, 1250, 1000, 1000, 12500, 12500, 1000, 1000, 12500, 12500, 1250, 12500, 1000])], axis=1)
        tbl_0 = 0.05 * jax.random.normal(jax.random.fold_in(_tk, 500 + 0), (1000, 128), jnp.float32)
        tbl_1 = 0.05 * jax.random.normal(jax.random.fold_in(_tk, 500 + 1), (1250, 128), jnp.float32)
        tbl_2 = 0.05 * jax.random.normal(jax.random.fold_in(_tk, 500 + 2), (125000, 128), jnp.float32)
        tbl_3 = 0.05 * jax.random.normal(jax.random.fold_in(_tk, 500 + 3), (1000, 128), jnp.float32)
        tbl_4 = 0.05 * jax.random.normal(jax.random.fold_in(_tk, 500 + 4), (1250, 128), jnp.float32)
        tbl_5 = 0.05 * jax.random.normal(jax.random.fold_in(_tk, 500 + 5), (1250, 128), jnp.float32)
        tbl_6 = 0.05 * jax.random.normal(jax.random.fold_in(_tk, 500 + 6), (1250, 128), jnp.float32)
        tbl_7 = 0.05 * jax.random.normal(jax.random.fold_in(_tk, 500 + 7), (1250, 128), jnp.float32)
        tbl_8 = 0.05 * jax.random.normal(jax.random.fold_in(_tk, 500 + 8), (1250, 128), jnp.float32)
        tbl_9 = 0.05 * jax.random.normal(jax.random.fold_in(_tk, 500 + 9), (1250, 128), jnp.float32)
        tbl_10 = 0.05 * jax.random.normal(jax.random.fold_in(_tk, 500 + 10), (1250, 128), jnp.float32)
        tbl_11 = 0.05 * jax.random.normal(jax.random.fold_in(_tk, 500 + 11), (12500, 128), jnp.float32)
        tbl_12 = 0.05 * jax.random.normal(jax.random.fold_in(_tk, 500 + 12), (1250, 128), jnp.float32)
        tbl_13 = 0.05 * jax.random.normal(jax.random.fold_in(_tk, 500 + 13), (1250, 128), jnp.float32)
        tbl_14 = 0.05 * jax.random.normal(jax.random.fold_in(_tk, 500 + 14), (1250, 128), jnp.float32)
        tbl_15 = 0.05 * jax.random.normal(jax.random.fold_in(_tk, 500 + 15), (1000, 128), jnp.float32)
        tbl_16 = 0.05 * jax.random.normal(jax.random.fold_in(_tk, 500 + 16), (1000, 128), jnp.float32)
        tbl_17 = 0.05 * jax.random.normal(jax.random.fold_in(_tk, 500 + 17), (12500, 128), jnp.float32)
        tbl_18 = 0.05 * jax.random.normal(jax.random.fold_in(_tk, 500 + 18), (12500, 128), jnp.float32)
        tbl_19 = 0.05 * jax.random.normal(jax.random.fold_in(_tk, 500 + 19), (1000, 128), jnp.float32)
        tbl_20 = 0.05 * jax.random.normal(jax.random.fold_in(_tk, 500 + 20), (1000, 128), jnp.float32)
        tbl_21 = 0.05 * jax.random.normal(jax.random.fold_in(_tk, 500 + 21), (12500, 128), jnp.float32)
        tbl_22 = 0.05 * jax.random.normal(jax.random.fold_in(_tk, 500 + 22), (12500, 128), jnp.float32)
        tbl_23 = 0.05 * jax.random.normal(jax.random.fold_in(_tk, 500 + 23), (1250, 128), jnp.float32)
        tbl_24 = 0.05 * jax.random.normal(jax.random.fold_in(_tk, 500 + 24), (12500, 128), jnp.float32)
        tbl_25 = 0.05 * jax.random.normal(jax.random.fold_in(_tk, 500 + 25), (1000, 128), jnp.float32)
        _rk = jax.random.fold_in(_tk, 7)
        r_dense_features = -0.000520686 + 1.00062 * jax.random.normal(jax.random.fold_in(_rk, 101), (512, 128), jnp.float32)
        W_top1 = 0.0405887 * jax.random.normal(jax.random.fold_in(_tk, 801), (607, 512), jnp.float32)
        W_top2 = 0.0441942 * jax.random.normal(jax.random.fold_in(_tk, 802), (512, 256), jnp.float32)
        W_top3 = 0.0625 * jax.random.normal(jax.random.fold_in(_tk, 803), (256, 1), jnp.float32)
        b_top1 = jnp.zeros((512,), jnp.float32)
        b_top2 = jnp.zeros((256,), jnp.float32)
        return (r_dense_features, ids, tbl_0, tbl_1, tbl_2, tbl_3, tbl_4, tbl_5, tbl_6, tbl_7, tbl_8, tbl_9, tbl_10, tbl_11, tbl_12, tbl_13, tbl_14, tbl_15, tbl_16, tbl_17, tbl_18, tbl_19, tbl_20, tbl_21, tbl_22, tbl_23, tbl_24, tbl_25, W_top1, b_top1, W_top2, b_top2, W_top3)
    r_dense_features, ids, tbl_0, tbl_1, tbl_2, tbl_3, tbl_4, tbl_5, tbl_6, tbl_7, tbl_8, tbl_9, tbl_10, tbl_11, tbl_12, tbl_13, tbl_14, tbl_15, tbl_16, tbl_17, tbl_18, tbl_19, tbl_20, tbl_21, tbl_22, tbl_23, tbl_24, tbl_25, W_top1, b_top1, W_top2, b_top2, W_top3 = _rec_inputs()

    def _L0_rec_setup():
        import jax, jax.numpy as jnp
        import numpy as np
        NUM_SPARSE = 26
        EMBED_DIM = 128
        BATCH = 2048
        key = jax.random.key(seed)
        k1, k2 = jax.random.split(key)
        dense_features = jax.random.normal(k1, (BATCH, EMBED_DIM), dtype=jnp.float32)
        sparse_features = jax.random.normal(k2, (BATCH, NUM_SPARSE, EMBED_DIM), dtype=jnp.float32)
        return {'dense_features': dense_features, 'sparse_features': sparse_features}
    _L0_rec_all = _L0_rec_setup()
    _L0_rec_in = {k: v for k, v in _L0_rec_all.items() if k in ()}
    del _L0_rec_all
    return {'r_dense_features': r_dense_features, 'ids': ids, 'tbl_0': tbl_0, 'tbl_1': tbl_1, 'tbl_2': tbl_2, 'tbl_3': tbl_3, 'tbl_4': tbl_4, 'tbl_5': tbl_5, 'tbl_6': tbl_6, 'tbl_7': tbl_7, 'tbl_8': tbl_8, 'tbl_9': tbl_9, 'tbl_10': tbl_10, 'tbl_11': tbl_11, 'tbl_12': tbl_12, 'tbl_13': tbl_13, 'tbl_14': tbl_14, 'tbl_15': tbl_15, 'tbl_16': tbl_16, 'tbl_17': tbl_17, 'tbl_18': tbl_18, 'tbl_19': tbl_19, 'tbl_20': tbl_20, 'tbl_21': tbl_21, 'tbl_22': tbl_22, 'tbl_23': tbl_23, 'tbl_24': tbl_24, 'tbl_25': tbl_25, 'W_top1': W_top1, 'b_top1': b_top1, 'W_top2': W_top2, 'b_top2': b_top2, 'W_top3': W_top3}

def reference(r_dense_features, ids, tbl_0, tbl_1, tbl_2, tbl_3, tbl_4, tbl_5, tbl_6, tbl_7, tbl_8, tbl_9, tbl_10, tbl_11, tbl_12, tbl_13, tbl_14, tbl_15, tbl_16, tbl_17, tbl_18, tbl_19, tbl_20, tbl_21, tbl_22, tbl_23, tbl_24, tbl_25, W_top1, b_top1, W_top2, b_top2, W_top3):
    import jax
    import jax.numpy as jnp

    def _L0_rec_ref(dense_features, sparse_features):
        import jax, jax.numpy as jnp
        import numpy as np
        NUM_SPARSE = 26
        EMBED_DIM = 128
        BATCH = 2048
        F = NUM_SPARSE + 1
        combined = jnp.concatenate([dense_features[:, None, :], sparse_features], axis=1)
        interactions = jnp.einsum('bfd,bgd->bfg', combined, combined)
        iu, ju = jnp.triu_indices(F, k=1)
        interactions_flat = interactions[:, iu, ju]
        return jnp.concatenate([dense_features, interactions_flat], axis=1)
    e = jnp.stack([tbl_0[ids[:, 0]], tbl_1[ids[:, 1]], tbl_2[ids[:, 2]], tbl_3[ids[:, 3]], tbl_4[ids[:, 4]], tbl_5[ids[:, 5]], tbl_6[ids[:, 6]], tbl_7[ids[:, 7]], tbl_8[ids[:, 8]], tbl_9[ids[:, 9]], tbl_10[ids[:, 10]], tbl_11[ids[:, 11]], tbl_12[ids[:, 12]], tbl_13[ids[:, 13]], tbl_14[ids[:, 14]], tbl_15[ids[:, 15]], tbl_16[ids[:, 16]], tbl_17[ids[:, 17]], tbl_18[ids[:, 18]], tbl_19[ids[:, 19]], tbl_20[ids[:, 20]], tbl_21[ids[:, 21]], tbl_22[ids[:, 22]], tbl_23[ids[:, 23]], tbl_24[ids[:, 24]], tbl_25[ids[:, 25]]], axis=1)
    z = _L0_rec_ref(r_dense_features, e)
    z = z.reshape(z.shape[0], -1)
    h = jnp.concatenate([z, r_dense_features], axis=1)
    h = jnp.maximum(h @ W_top1 + b_top1, 0.0)
    h = jnp.maximum(h @ W_top2 + b_top2, 0.0)
    y = h @ W_top3
    return y

_drawn_inputs = setup_inputs


def setup_inputs(seed=0):
    import zlib

    import numpy as np

    out = dict(_drawn_inputs(seed))
    spreads = {'b_top1': (0.0, 0.1), 'b_top2': (0.0, 0.1)}
    factors = {}
    for name, (base, spread) in spreads.items():
        noise = np.random.default_rng([zlib.crc32(name.encode()), seed]).standard_normal(out[name].shape)
        drawn = base * np.exp(spread * noise) if base else spread * noise
        out[name] = jnp.asarray(drawn.astype(out[name].dtype))
    for name, factor in factors.items():
        out[name] = (out[name] * factor).astype(out[name].dtype)
    return out
```

```python
from contextlib import ExitStack

import concourse.bass as bass
from concourse import mybir

F32 = mybir.dt.float32
I32 = mybir.dt.int32
ALU = mybir.AluOpType
ACT = mybir.ActivationFunctionType

P = 128


def dlrm_tower(nc, dense, ids, tables, W_top1, b_top1, W_top2, b_top2, W_top3, out):
    B, D = dense.shape
    T = len(tables)
    F = T + 1
    NT = B // P
    N1, N2 = W_top1.shape[1], W_top2.shape[1]
    C1, C2 = N1 // P, N2 // P
    M = F - 1
    PAIRS = F * (F - 1) // 2
    ZC = 3
    ZP = PAIRS // ZC
    XG = 4
    NX = (F + XG - 1) // XG
    XD, XA = (NX + 1) // 2, NX // 2
    GS = 16
    NG = P // GS
    assert D == P and ZP * ZC == PAIRS and ZP <= P and GS * M <= 512 and N1 <= 512 and NT % 2 == 0

    def slots(g):
        return range(XG * g, min(XG * g + XG, F))

    def pair_start(f):
        return f * (F - 1) - f * (f - 1) // 2

    with ExitStack() as ctx:
        def sb(name, shape, dt=F32):
            return ctx.enter_context(nc.sbuf_tensor(name, shape, dt))

        def ps(name):
            return ctx.enter_context(nc.psum_tensor(name, [P, 512], F32))

        def sem(name):
            return ctx.enter_context(nc.semaphore(name))

        ident = sb("ident", [P, P])
        anti = sb("anti", [M, M])
        ids_sb = sb("ids_sb", [P, NT, T], I32)
        rows = sb("rows", [P, 2, F, D])
        xt = sb("xt", [D, P, F])
        gram = sb("gram", [M, P, M])
        z = sb("z", [P, PAIRS])
        zt = sb("zt", [ZP, ZC, P])
        dense_t = sb("dense_t", [D, P])
        h1 = sb("h1", [P, C1, P])
        h2 = sb("h2", [P, C2, P])
        w1_first = sb("w1_first", [D, N1])
        w1_last = sb("w1_last", [D, N1])
        w1_pairs = sb("w1_pairs", [ZP, ZC, N1])
        w2 = sb("w2", [P, C1, N2])
        w3 = sb("w3", [P, C2])
        b1 = sb("b1", [P, C1])
        b2 = sb("b2", [P, C2])
        y = sb("y", [1, B])

        x_bank = [ps("x_bank0"), ps("x_bank1")]
        g_bank = [ps("g_bank0"), ps("g_bank1")]
        z_bank = ps("z_bank")
        h_bank = [ps("h_bank0"), ps("h_bank1")]
        y_bank = ps("y_bank")

        ids_loaded = sem("ids_loaded")
        consts_cleared = sem("consts_cleared")
        consts_ready = sem("consts_ready")
        gathered = [[sem(f"gathered{p}_{g}") for g in range(NX)] for p in range(2)]
        dense_loaded = [sem("dense_loaded0"), sem("dense_loaded1")]
        w1_loaded = sem("w1_loaded")
        w2_loaded = sem("w2_loaded")
        w3_loaded = sem("w3_loaded")
        bias_loaded = sem("bias_loaded")
        x_turned = sem("x_turned")
        x_copied_v = sem("x_copied_v")
        x_copied_s = sem("x_copied_s")
        dense_copied = sem("dense_copied")
        g_ready = sem("g_ready")
        g_copied_v = sem("g_copied_v")
        g_copied_s = sem("g_copied_s")
        z_ready = sem("z_ready")
        z_copied = sem("z_copied")
        zt_ready = sem("zt_ready")
        zt_copied = sem("zt_copied")
        h1_ready_v = sem("h1_ready_v")
        h1_ready_s = sem("h1_ready_s")
        h1_copied_v = sem("h1_copied_v")
        h1_copied_s = sem("h1_copied_s")
        h2_ready_v = sem("h2_ready_v")
        h2_ready_s = sem("h2_ready_s")
        h2_copied_v = sem("h2_copied_v")
        h2_copied_s = sem("h2_copied_s")
        y_ready = sem("y_ready")
        y_copied = sem("y_copied")
        y_stored = sem("y_stored")

        def h1_out(c):
            return h_bank[c % 2][:, c // 2 * P:c // 2 * P + P]

        def h2_out(c):
            return h_bank[c % 2][:, 2 * P:3 * P]

        block = ctx.enter_context(nc.Block())

        @block.sync
        def _(sp):
            sp.dma_start(ids_sb[:], ids.rearrange("(t p) f -> p t f", p=P)).then_inc(ids_loaded, 16)
            for t in range(2):
                sp.dma_start(rows[:, t, F - 1, :], dense[t * P:t * P + P, :]).then_inc(dense_loaded[t], 16)
            zw = W_top1[D:D + PAIRS, :].rearrange("(c p) n -> p c n", c=ZC)
            sp.dma_start(w1_first[:], W_top1[0:D, :]).then_inc(w1_loaded, 16)
            sp.dma_start(w1_last[:], W_top1[D + PAIRS:D + PAIRS + D, :]).then_inc(w1_loaded, 16)
            sp.dma_start(w1_pairs[:], zw).then_inc(w1_loaded, 16)
            sp.dma_start(w2[:], W_top2.rearrange("(c p) n -> p c n", c=C1)).then_inc(w2_loaded, 16)
            with nc.allow_non_contiguous_dma(reason="columns of a few hundred words, once"):
                sp.dma_start(b1[:], b_top1.rearrange("(c p) -> p c", c=C1)).then_inc(bias_loaded, 16)
                sp.dma_start(b2[:], b_top2.rearrange("(c p) -> p c", c=C2)).then_inc(bias_loaded, 16)
                sp.dma_start(w3[:], W_top3.rearrange("(c p) o -> p (c o)", c=C2)).then_inc(w3_loaded, 16)
            for t in range(2, NT):
                sp.wait_ge(x_turned, NX * (t - 1))
                sp.dma_start(rows[:, t % 2, F - 1, :], dense[t * P:t * P + P, :]).then_inc(dense_loaded[t % 2], 16)
            sp.wait_ge(y_copied, 1)
            sp.dma_start(out.rearrange("n o -> o n"), y[:]).then_inc(y_stored, 16)
            sp.wait_ge(y_stored, 16)

        @block.gpsimd
        def _(pool):
            nc.gpsimd.memset(ident[:], 0.0).then_inc(consts_cleared, 1)
            nc.gpsimd.memset(anti[:], 0.0).then_inc(consts_cleared, 1)
            pool.wait_ge(consts_cleared, 2)
            nc.gpsimd.affine_select(out=ident[:], in_=ident[:], compare_op=ALU.not_equal, fill=1.0, base=0,
                                    pattern=[[-1, P]], channel_multiplier=1).then_inc(consts_ready, 1)
            nc.gpsimd.affine_select(out=anti[:], in_=anti[:], compare_op=ALU.not_equal, fill=1.0,
                                    base=-(M - 1), pattern=[[1, M]], channel_multiplier=1).then_inc(consts_ready, 1)
            pool.wait_ge(ids_loaded, 16)
            for t in range(NT):
                if t >= 2:
                    pool.wait_ge(x_turned, NX * (t - 1))
                for r in range(T):
                    f = T - 1 - r
                    pool.indirect_dma_start(
                        rows[:, t % 2, r, :], None, tables[f],
                        bass.IndirectOffsetOnAxis(ids_sb[:, t, f:f + 1], 0),
                    ).then_inc(gathered[t % 2][r // XG], 16)

        @block.tensor
        def _(pe):
            def turn_rows(p, i):
                t = 2 * i + p
                pe.wait_ge(dense_loaded[p], 16 * i + 16)
                for g in range(NX):
                    n = sum(r < T for r in slots(g))
                    pe.wait_ge(gathered[p][g], 16 * n * i + 16 * n)
                    if g >= 2:
                        pe.wait_ge(x_copied_s if g % 2 else x_copied_v, (XA if g % 2 else XD) * t + g // 2)
                    for r in slots(g):
                        k = r - XG * g
                        mm = pe.transpose(x_bank[g % 2][:, k * P:k * P + P], rows[:, p, r, :], ident[:])
                    mm.then_inc(x_turned, 1)

            def interact(p, i):
                t = 2 * i + p
                pe.wait_ge(x_copied_v, XD * t + XD)
                pe.wait_ge(x_copied_s, XA * t + XA)
                for g in range(NG):
                    if g >= 2:
                        pe.wait_ge(g_copied_s if g % 2 else g_copied_v, NG // 2 * t + g // 2)
                    for k in range(GS):
                        s = GS * g + k
                        mm = pe.matmul(g_bank[g % 2][0:M, k * M:k * M + M], xt[:, s, 0:M], xt[:, s, 1:F],
                                       start=True, stop=True)
                    mm.then_inc(g_ready, 1)

            def pairs(p, i):
                for f in range(F - 1):
                    n = F - 1 - f
                    at = pair_start(f)
                    mm = pe.transpose(z_bank[:, at:at + n], gram[0:n, :, F - 2 - f], anti[0:n, M - n:M])
                mm.then_inc(z_ready, 1)

            def layer1_dense(p, i):
                t = 2 * i + p
                pe.wait_ge(dense_copied, t + 1)
                for c in range(C1):
                    pe.matmul(h1_out(c), w1_first[:, c * P:c * P + P], dense_t[:], start=(c < 2), stop=False,
                              skip_group_check=True)
                    if c == C1 - 1:
                        pe.wait_ge(g_copied_v, NG // 2 * t + NG // 2)
                        pe.wait_ge(g_copied_s, NG // 2 * t + NG // 2)
                    pe.matmul(h1_out(c), w1_last[:, c * P:c * P + P], dense_t[:], start=False, stop=False,
                              skip_group_check=True)

            def layer1_pairs(p, i):
                t = 2 * i + p
                pe.wait_ge(z_copied, t + 1)
                for c in range(ZC):
                    mm = pe.transpose(z_bank[0:ZP, c * P:c * P + P], z[:, c * ZP:c * ZP + ZP], ident[:])
                mm.then_inc(zt_ready, 1)
                pe.wait_ge(zt_copied, t + 1)
                for bank, ready in ((0, h1_ready_v), (1, h1_ready_s)):
                    for c in range(bank, C1, 2):
                        for k in range(ZC):
                            mm = pe.matmul(h1_out(c), w1_pairs[:, k, c * P:c * P + P], zt[:, k, :],
                                           start=False, stop=(k == ZC - 1), skip_group_check=True)
                    mm.then_inc(ready, 1)

            def layers23(p, i):
                t = 2 * i + p
                for c, ready in ((0, h2_ready_v), (1, h2_ready_s)):
                    for bank, copied in ((0, h1_copied_v), (1, h1_copied_s)):
                        pe.wait_ge(copied, t + 1)
                        for k in range(bank, C1, 2):
                            mm = pe.matmul(h2_out(c), w2[:, k, c * P:c * P + P], h1[:, k, :],
                                           start=(k == 0), stop=(k == C1 - 1))
                    mm.then_inc(ready, 1)
                pe.wait_ge(h2_copied_v, t + 1)
                pe.wait_ge(h2_copied_s, t + 1)
                for k in range(C2):
                    mm = pe.matmul(y_bank[0:1, bass.ts(t, P)], w3[:, k:k + 1], h2[:, k, :], start=(k == 0), stop=(k == C2 - 1))
                mm.then_inc(y_ready, 1)

            pe.wait_ge(consts_ready, 2)
            pe.wait_ge(w1_loaded, 48)
            pe.wait_ge(w2_loaded, 16)
            pe.wait_ge(w3_loaded, 16)
            with nc.tensor.Fori(0, NT // 2) as i:
                for p in range(2):
                    turn_rows(p, i)
                    interact(p, i)
                    layer1_dense(p, i)
                    pairs(p, i)
                    layer1_pairs(p, i)
                    layers23(p, i)

        @block.vector
        def _(dve):
            dve.wait_ge(bias_loaded, 32)
            with nc.vector.Fori(0, NT) as t:
                for g in range(0, NX, 2):
                    dve.wait_ge(x_turned, NX * t + g + 1)
                    n = len(slots(g))
                    nc.vector.tensor_copy(
                        xt[:, :, XG * g:XG * g + n].rearrange("d s r -> d r s"),
                        x_bank[0][:, 0:n * P].rearrange("d (r s) -> d r s", r=n),
                    ).then_inc(x_copied_v, 1)
                for g in range(0, NG, 2):
                    dve.wait_ge(g_ready, NG * t + g + 1)
                    nc.vector.tensor_copy(gram[:, GS * g:GS * g + GS, :],
                                          g_bank[0][0:M, 0:GS * M].rearrange("r (s f) -> r s f", f=M),
                                          ).then_inc(g_copied_v, 1)
                dve.wait_ge(z_ready, t + 1)
                nc.vector.tensor_copy(z[:], z_bank[:, 0:PAIRS]).then_inc(z_copied, 1)
                dve.wait_ge(h1_ready_v, t + 1)
                for c in range(0, C1, 2):
                    op = nc.vector.tensor_scalar(h1[:, c, :], h1_out(c), b1[:, c:c + 1], 0.0, ALU.add, ALU.max)
                op.then_inc(h1_copied_v, 1)
                dve.wait_ge(h2_ready_v, t + 1)
                nc.vector.tensor_scalar(h2[:, 0, :], h2_out(0), b2[:, 0:1], 0.0, ALU.add,
                                        ALU.max).then_inc(h2_copied_v, 1)
            dve.wait_ge(y_ready, NT)
            nc.vector.tensor_copy(y[:], y_bank[0:1, 0:B]).then_inc(y_copied, 1)

        @block.scalar
        def _(act):
            act.wait_ge(bias_loaded, 32)
            with nc.scalar.Fori(0, NT) as t:
                for g in range(1, NX, 2):
                    act.wait_ge(x_turned, NX * t + g + 1)
                    n = len(slots(g))
                    nc.scalar.copy(
                        xt[:, :, XG * g:XG * g + n].rearrange("d s r -> d r s"),
                        x_bank[1][:, 0:n * P].rearrange("d (r s) -> d r s", r=n),
                    ).then_inc(x_copied_s, 1)
                act.wait_ge(x_copied_v, XD * t + XD)
                nc.scalar.copy(dense_t[:], xt[:, :, F - 1]).then_inc(dense_copied, 1)
                for g in range(1, NG, 2):
                    act.wait_ge(g_ready, NG * t + g + 1)
                    nc.scalar.copy(gram[:, GS * g:GS * g + GS, :],
                                   g_bank[1][0:M, 0:GS * M].rearrange("r (s f) -> r s f", f=M),
                                   ).then_inc(g_copied_s, 1)
                act.wait_ge(zt_ready, t + 1)
                nc.scalar.copy(zt[:], z_bank[0:ZP, 0:ZC * P].rearrange("r (c s) -> r c s", c=ZC)).then_inc(zt_copied, 1)
                act.wait_ge(h1_ready_s, t + 1)
                for c in range(1, C1, 2):
                    op = nc.scalar.activation(h1[:, c, :], h1_out(c), ACT.Relu, bias=b1[:, c:c + 1])
                op.then_inc(h1_copied_s, 1)
                act.wait_ge(h2_ready_s, t + 1)
                nc.scalar.activation(h2[:, 1, :], h2_out(1), ACT.Relu, bias=b2[:, 1:2]).then_inc(h2_copied_s, 1)


def kernel(**inputs):
    import numpy as np
    import concourse.bacc as bacc
    from concourse import mybir as _mybir
    from concourse.bass_utils import run_bass_kernel_spmd

    nc = bacc.Bacc("TRN2", target_bir_lowering=False, num_devices=1)
    arrays, args = {}, {}
    for name, value in inputs.items():
        a = np.ascontiguousarray(value)
        arrays[f"in_{name}"] = a
        args[name] = nc.dram_tensor(f"in_{name}", a.shape, _mybir.dt.from_np(a.dtype), kind="ExternalInput").ap()
    samples = inputs["r_dense_features"].shape[0]
    out = nc.dram_tensor("out_y", (samples, 1), _mybir.dt.float32, kind="ExternalOutput").ap()
    tables = [args[f"tbl_{f}"] for f in range(inputs["ids"].shape[1])]
    dlrm_tower(nc, args["r_dense_features"], args["ids"], tables, args["W_top1"], args["b_top1"],
               args["W_top2"], args["b_top2"], args["W_top3"], out)
    r = run_bass_kernel_spmd(nc, [arrays], core_ids=[0])
    return r.results[0]["out_y"]
```

```python
from contextlib import ExitStack

import concourse.bass as bass
from concourse import mybir

F32 = mybir.dt.float32
F32R = mybir.dt.float32r
F16 = mybir.dt.float16
I32 = mybir.dt.int32
ALU = mybir.AluOpType
ACT = mybir.ActivationFunctionType

P = 128


def dlrm_tower(nc, dense, ids, tables, W_top1, b_top1, W_top2, b_top2, W_top3, out):
    B, D = dense.shape
    T = len(tables)
    F = T + 1
    NT = B // P
    N1, N2 = W_top1.shape[1], W_top2.shape[1]
    C1, C2 = N1 // P, N2 // P
    M = F - 1
    PAIRS = F * (F - 1) // 2
    ZC = 3
    ZP = PAIRS // ZC
    GS = 16
    NG = P // GS
    TC = 8
    TV = 6

    small = [f for f in range(T) if tables[f].shape[0] <= TC * P and tables[f].shape[0] % TC == 0]
    TR = tables[small[0]].shape[0] // TC
    small = [f for f in small if tables[f].shape[0] == TR * TC][:6]
    K = len(small)
    small_slot = [T - 1 - f for f in small]
    turned = [r for r in range(1, F) if r not in small_slot] + [0]
    groups = [turned[n:n + 4] for n in range(0, len(turned), 4)]
    NX = len(groups)
    XD, XA = NX - NX // 2, NX // 2
    dense_group = next(g for g in range(NX) if F - 1 in groups[g])
    assert D == P and ZP * ZC == PAIRS and ZP <= P and GS * M <= 512 and N1 <= 512 and NT % 2 == 0
    assert K % 2 == 0 and K <= 6 and TR * TC <= 2048 and B <= 512 and 0 not in small_slot and dense_group % 2 == 0

    first_groups = [[], [0], [1], [2], [3], [4, 5]]

    def runs(group):
        found = []
        for k, r in enumerate(group):
            if found and r == found[-1][0] + found[-1][2]:
                found[-1][2] += 1
            else:
                found.append([r, k, 1])
        return found

    def pair_start(f):
        return f * (F - 1) - f * (f - 1) // 2

    with ExitStack() as ctx:
        def sb(name, shape, dt=F32):
            return ctx.enter_context(nc.sbuf_tensor(name, shape, dt))

        def ps(name):
            return ctx.enter_context(nc.psum_tensor(name, [P, 512], F32))

        def sem(name):
            return ctx.enter_context(nc.semaphore(name))

        ident = sb("ident", [P, P])
        anti = sb("anti", [M, M])
        row_of = sb("row_of", [TR, TC])
        ids_sb = sb("ids_sb", [P, NT, T], I32)
        ids_f = sb("ids_f", [P, NT, K])
        ids_t = sb("ids_t", [K, B], F16)
        pick = sb("pick", [K, K, TR], F16)
        ids_wide = sb("ids_wide", [TR, K * B])
        table = sb("table", [TR, 2, TC * D])
        table_hi = sb("table_hi", [TR, 2, TC * D], F32R)
        table_lo = sb("table_lo", [TR, 2, TC * D], F32R)
        distance = sb("distance", [TR, 2, B])
        hot = sb("hot", [TR, 2, TC, B], F32R)
        small_rows = sb("small_rows", [D, K * B])
        rows = sb("rows", [P, 2, F, D])
        xt = sb("xt", [D, P, F])
        gram = sb("gram", [M, P, M])
        z = sb("z", [P, PAIRS])
        zt = sb("zt", [ZP, ZC, P])
        dense_t = sb("dense_t", [D, P])
        h1 = sb("h1", [P, C1, P])
        h2 = sb("h2", [P, C2, P])
        w1_first = sb("w1_first", [D, N1])
        w1_last = sb("w1_last", [D, N1])
        w1_dense = sb("w1_dense", [D, N1])
        w1_pairs = sb("w1_pairs", [ZP, ZC, N1])
        w2 = sb("w2", [P, C1, N2])
        w3 = sb("w3", [P, C2])
        b1 = sb("b1", [P, C1])
        b2 = sb("b2", [P, C2])
        y = sb("y", [1, B])

        x_bank = [ps("x_bank0"), ps("x_bank1")]
        g_bank = [ps("g_bank0"), ps("g_bank1")]
        z_bank = ps("z_bank")
        h_bank = [ps("h_bank0"), ps("h_bank1")]
        y_bank = ps("y_bank")
        spread_bank = [z_bank, y_bank, *h_bank, *x_bank]

        def h1_out(c):
            return h_bank[c % 2][:, c // 2 * P:c // 2 * P + P]

        h2_out = [h_bank[0][:, 3 * P:4 * P], z_bank[:, ZC * P:ZC * P + P]]
        assert C2 == 2 and C1 == 4 and ZC == 3

        ids_loaded = sem("ids_loaded")
        consts_cleared = sem("consts_cleared")
        consts_ready = sem("consts_ready")
        ids_float = sem("ids_float")
        ids_turned = sem("ids_turned")
        ids_t_ready = sem("ids_t_ready")
        ids_spread = sem("ids_spread")
        ids_wide_ready = sem("ids_wide_ready")
        table_loaded = [sem("table_loaded0"), sem("table_loaded1")]
        act_warm = sem("act_warm")
        hi_ready = sem("hi_ready")
        lo_ready = sem("lo_ready")
        distance_ready = sem("distance_ready")
        hot_ready_v = sem("hot_ready_v")
        hot_ready_s = sem("hot_ready_s")
        small_summed = sem("small_summed")
        small_copied = sem("small_copied")
        gathered = [[sem(f"gathered{p}_{g}") for g in range(NX)] for p in range(2)]
        dense_loaded = [sem("dense_loaded0"), sem("dense_loaded1")]
        w1_loaded = sem("w1_loaded")
        w1_dense_ready = sem("w1_dense_ready")
        weights_loaded = sem("weights_loaded")
        x_turned = sem("x_turned")
        x_ready = [sem("x_ready_v"), sem("x_ready_s")]
        small_placed = [sem("small_placed_v"), sem("small_placed_s")]
        dense_ready = sem("dense_ready")
        g_summed = sem("g_summed")
        g_copied = [sem("g_copied_v"), sem("g_copied_s")]
        z_turned = sem("z_turned")
        z_copied = sem("z_copied")
        zt_turned = sem("zt_turned")
        zt_copied = sem("zt_copied")
        h1_summed = [sem("h1_summed0"), sem("h1_summed1")]
        h1_ready = [sem("h1_ready_v"), sem("h1_ready_s")]
        h2_summed = [sem("h2_summed0"), sem("h2_summed1")]
        h2_ready = [sem("h2_ready_v"), sem("h2_ready_s")]
        y_summed = sem("y_summed")
        y_ready = sem("y_ready")
        y_stored = sem("y_stored")

        block = ctx.enter_context(nc.Block())

        @block.sync
        def _(sp):
            def load_table(i):
                sp.dma_start(table[:, i % 2, :], tables[small[i]].rearrange("(p c) d -> p (c d)", c=TC),
                             ).then_inc(table_loaded[i % 2], 16)

            def load_dense(t):
                sp.dma_start(rows[:, t % 2, F - 1, :], dense[t * P:t * P + P, :]).then_inc(dense_loaded[t % 2], 16)

            sp.dma_start(ids_sb[:], ids.rearrange("(t p) f -> p t f", p=P)).then_inc(ids_loaded, 16)
            load_table(0)
            load_table(1)
            load_dense(0)
            load_dense(1)
            sp.dma_start(w1_first[:], W_top1[0:D, :]).then_inc(w1_loaded, 16)
            sp.dma_start(w1_last[:], W_top1[D + PAIRS:D + PAIRS + D, :]).then_inc(w1_loaded, 16)
            for i in range(2, K):
                sp.wait_ge(hi_ready, i - 1)
                sp.wait_ge(lo_ready, i - 1)
                load_table(i)
                if i == 2:
                    sp.dma_start(w1_pairs[:], W_top1[D:D + PAIRS, :].rearrange("(c p) n -> p c n", c=ZC),
                                 ).then_inc(weights_loaded, 16)
                    sp.dma_start(w2[:], W_top2.rearrange("(c p) n -> p c n", c=C1)).then_inc(weights_loaded, 16)
                    with nc.allow_non_contiguous_dma(reason="columns of a few hundred words, once"):
                        sp.dma_start(b1[:], b_top1.rearrange("(c p) -> p c", c=C1)).then_inc(weights_loaded, 16)
                        sp.dma_start(b2[:], b_top2.rearrange("(c p) -> p c", c=C2)).then_inc(weights_loaded, 16)
                        sp.dma_start(w3[:], W_top3.rearrange("(c p) o -> p (c o)", c=C2),
                                     ).then_inc(weights_loaded, 16)
            for t in range(2, NT):
                sp.wait_ge(x_turned, NX * (t - 1))
                load_dense(t)
            sp.wait_ge(y_ready, 1)
            sp.dma_start(out.rearrange("n o -> o n"), y[:]).then_inc(y_stored, 16)
            sp.wait_ge(y_stored, 16)

        @block.gpsimd
        def _(pool):
            nc.gpsimd.memset(ident[:], 0.0).then_inc(consts_cleared, 1)
            nc.gpsimd.memset(anti[:], 0.0).then_inc(consts_cleared, 1)
            pool.wait_ge(consts_cleared, 2)
            nc.gpsimd.affine_select(out=ident[:], in_=ident[:], compare_op=ALU.not_equal, fill=1.0, base=0,
                                    pattern=[[-1, P]], channel_multiplier=1).then_inc(consts_ready, 1)
            nc.gpsimd.affine_select(out=anti[:], in_=anti[:], compare_op=ALU.not_equal, fill=1.0,
                                    base=-(M - 1), pattern=[[1, M]], channel_multiplier=1).then_inc(consts_ready, 1)
            nc.gpsimd.iota(row_of[:], pattern=[[1, TC]], base=0, channel_multiplier=TC,
                           allow_small_or_imprecise_dtypes=True).then_inc(consts_ready, 1)
            pool.wait_ge(ids_loaded, 16)
            for t in range(NT):
                if t >= 2:
                    pool.wait_ge(x_turned, NX * (t - 1))
                for g in range(NX):
                    for r in groups[g]:
                        if r < T:
                            pool.indirect_dma_start(
                                rows[:, t % 2, r, :], None, tables[T - 1 - r],
                                bass.IndirectOffsetOnAxis(ids_sb[:, t, T - 1 - r:T - r], 0),
                            ).then_inc(gathered[t % 2][g], 16)

        @block.tensor
        def _(pe):
            def spread_ids():
                pe.wait_ge(consts_ready, 3)
                pe.wait_ge(ids_float, 1)
                for t in range(NT):
                    mm = pe.transpose(x_bank[0][0:K, t * P:t * P + P], ids_f[:, t, :], ident[:])
                mm.then_inc(ids_turned, 1)
                pe.wait_ge(ids_t_ready, 1)
                for i in range(K):
                    pe.matmul(spread_bank[i][0:TR, 0:B], pick[:, i, :], ids_t[:], start=True,
                              stop=True).then_inc(ids_spread, 1)

            def look_up(i, q):
                pe.wait_ge(hi_ready, i + 1)
                if i >= 2:
                    pe.wait_ge(small_copied, i - 1)
                for c in range(TC):
                    if c < TV:
                        pe.wait_ge(hot_ready_v, TV * i + c + 1)
                    else:
                        pe.wait_ge(hot_ready_s, (TC - TV) * i + c - TV + 1)
                    pe.matmul(g_bank[q][:, 0:B], table_hi[:, q, c * D:c * D + D], hot[:, q, c, :],
                              start=(c == 0), stop=False)
                pe.wait_ge(lo_ready, i + 1)
                for c in range(TC):
                    mm = pe.matmul(g_bank[q][:, 0:B], table_lo[:, q, c * D:c * D + D], hot[:, q, c, :],
                                   start=False, stop=(c == TC - 1))
                mm.then_inc(small_summed, 1)

            def turn_group(p, i, g):
                t = 2 * i + p
                n = sum(r < T for r in groups[g])
                pe.wait_ge(gathered[p][g], 16 * n * i + 16 * n)
                if g == dense_group:
                    pe.wait_ge(dense_loaded[p], 16 * i + 16)
                if g >= 2:
                    pe.wait_ge(x_ready[g % 2], (XD, XA)[g % 2] * t + g // 2)
                for k, r in enumerate(groups[g]):
                    mm = pe.transpose(x_bank[g % 2][:, k * P:k * P + P], rows[:, p, r, :], ident[:])
                mm.then_inc(x_turned, 1)

            def interact(p, i):
                t = 2 * i + p
                pe.wait_ge(small_placed[0], t + 1)
                pe.wait_ge(small_placed[1], t + 1)
                pe.wait_ge(x_ready[1], XA * t + XA)
                pe.wait_ge(x_ready[0], XD * t + XD)
                for g in range(NG):
                    if g >= 2:
                        pe.wait_ge(g_copied[g % 2], NG // 2 * t + g // 2)
                    for k in range(GS):
                        s = GS * g + k
                        mm = pe.matmul(g_bank[g % 2][0:M, k * M:k * M + M], xt[:, s, 0:M], xt[:, s, 1:F],
                                       start=True, stop=True)
                    mm.then_inc(g_summed, 1)

            def layer1_dense(p, i):
                t = 2 * i + p
                pe.wait_ge(dense_ready, t + 1)
                for c in range(C1):
                    if c == C1 - 1:
                        pe.wait_ge(g_copied[0], NG // 2 * t + NG // 2)
                        pe.wait_ge(g_copied[1], NG // 2 * t + NG // 2)
                    pe.matmul(h1_out(c), w1_dense[:, c * P:c * P + P], dense_t[:], start=(c < 2), stop=False,
                              skip_group_check=True)

            def pairs(p, i):
                for f in range(F - 1):
                    n = F - 1 - f
                    at = pair_start(f)
                    mm = pe.transpose(z_bank[:, at:at + n], gram[0:n, :, F - 2 - f], anti[0:n, M - n:M])
                mm.then_inc(z_turned, 1)

            def turn_pairs(p, i):
                t = 2 * i + p
                pe.wait_ge(z_copied, t + 1)
                for c in range(ZC):
                    mm = pe.transpose(z_bank[0:ZP, c * P:c * P + P], z[:, c * ZP:c * ZP + ZP], ident[:])
                mm.then_inc(zt_turned, 1)

            def layer1_pairs(p, i):
                t = 2 * i + p
                pe.wait_ge(zt_copied, t + 1)
                for bank in range(2):
                    for c in range(bank, C1, 2):
                        for k in range(ZC):
                            mm = pe.matmul(h1_out(c), w1_pairs[:, k, c * P:c * P + P], zt[:, k, :],
                                           start=False, stop=(k == ZC - 1), skip_group_check=True)
                    mm.then_inc(h1_summed[bank], 1)

            def layer2(p, i):
                t = 2 * i + p
                for half in range(2):
                    pe.wait_ge(h1_ready[half], t + 1)
                    for c in range(C2):
                        for k in range(half, C1, 2):
                            mm = pe.matmul(h2_out[c], w2[:, k, c * P:c * P + P], h1[:, k, :],
                                           start=(k == 0), stop=(k == C1 - 1))
                        if half == 1:
                            mm.then_inc(h2_summed[c], 1)

            def layer3(p, i):
                t = 2 * i + p
                pe.wait_ge(h2_ready[0], t + 1)
                pe.wait_ge(h2_ready[1], t + 1)
                for c in range(C2):
                    mm = pe.matmul(y_bank[0:1, bass.ts(t, P)], w3[:, c:c + 1], h2[:, c, :],
                                   start=(c == 0), stop=(c == C2 - 1))
                mm.then_inc(y_summed, 1)

            def finish_tile(p, i, between):
                layer1_dense(p, i)
                pairs(p, i)
                for step, gs in ((turn_pairs, (0,)), (layer1_pairs, (1,)), (layer2, (2,)), (layer3, (3,))):
                    if between:
                        for g in gs:
                            turn_group(1 - p, i + p, g)
                    step(p, i)
                if between:
                    for g in range(4, NX):
                        turn_group(1 - p, i + p, g)

            spread_ids()
            for i in range(K):
                look_up(i, i % 2)
                if i == 1:
                    pe.wait_ge(ids_wide_ready, K)
                for g in first_groups[i]:
                    turn_group(0, 0, g)
            pe.wait_ge(small_copied, K)
            for t in range(NT):
                interact(t % 2, t // 2)
                if t == 0:
                    pe.wait_ge(w1_dense_ready, 1)
                    pe.wait_ge(weights_loaded, 80)
                finish_tile(t % 2, t // 2, t + 1 < NT)

        def copy_group(eng_copy, g):
            for r, k, n in runs(groups[g]):
                op = eng_copy(
                    xt[:, :, r:r + n].rearrange("d s r -> d r s"),
                    x_bank[g % 2][:, k * P:(k + n) * P].rearrange("d (r s) -> d r s", r=n),
                )
            return op

        @block.vector
        def _(dve):
            dve.wait_ge(consts_ready, 3)
            for n in range(K):
                nc.vector.tensor_copy(pick[:, n, :], ident[0:K, n:n + 1].to_broadcast([K, TR]))
            dve.wait_ge(ids_loaded, 16)
            for f, n, m in runs(small):
                op = nc.vector.tensor_copy(ids_f[:, :, n:n + m], ids_sb[:, :, f:f + m])
            op.then_inc(ids_float, 1)
            dve.wait_ge(ids_turned, 1)
            nc.vector.tensor_copy(ids_t[:], x_bank[0][0:K, 0:B]).then_inc(ids_t_ready, 1)

            def split_and_mark(i, q):
                if i >= 2:
                    dve.wait_ge(small_summed, i - 1)
                dve.wait_ge(ids_wide_ready, i + 1)
                for c in range(TV):
                    nc.vector.tensor_scalar(hot[:, q, c, :], ids_wide[:, bass.ts(i, B)], row_of[:, c:c + 1], None,
                                            ALU.is_equal).then_inc(hot_ready_v, 1)
                dve.wait_ge(hi_ready, i + 1)
                nc.vector.tensor_tensor(table_lo[:, q, :], table[:, q, :], table_hi[:, q, :].bitcast(F32),
                                        ALU.subtract).then_inc(lo_ready, 1)

            def place(t, g):
                dve.wait_ge(x_turned, NX * t + g + 1)
                copy_group(nc.vector.tensor_copy, g).then_inc(x_ready[0], 1)
                if g == 0 and t > 0:
                    place_small(t)

            def place_small(t):
                dve.wait_ge(small_copied, K)
                for n in range(0, K, 2):
                    op = nc.vector.tensor_copy(xt[:, :, small_slot[n]], small_rows[:, n * B + P * t:n * B + P * t + P])
                op.then_inc(small_placed[0], 1)

            def keep_products(t):
                for g in range(0, NG, 2):
                    dve.wait_ge(g_summed, NG * t + g + 1)
                    nc.vector.tensor_copy(gram[:, GS * g:GS * g + GS, :],
                                          g_bank[0][0:M, 0:GS * M].rearrange("r (s f) -> r s f", f=M),
                                          ).then_inc(g_copied[0], 1)

            def finish_tile(t, between):
                dve.wait_ge(z_turned, t + 1)
                nc.vector.tensor_copy(z[:], z_bank[:, 0:PAIRS]).then_inc(z_copied, 1)
                if between:
                    place(t + 1, 0)
                dve.wait_ge(h1_summed[0], t + 1)
                for c in range(0, C1, 2):
                    op = nc.vector.tensor_scalar(h1[:, c, :], h1_out(c), b1[:, c:c + 1], 0.0, ALU.add, ALU.max)
                op.then_inc(h1_ready[0], 1)
                if between:
                    place(t + 1, 2)
                dve.wait_ge(h2_summed[0], t + 1)
                nc.vector.tensor_scalar(h2[:, 0, :], h2_out[0], b2[:, 0:1], 0.0, ALU.add,
                                        ALU.max).then_inc(h2_ready[0], 1)
                if between:
                    for g in range(4, NX, 2):
                        place(t + 1, g)

            for i in range(K):
                split_and_mark(i, i % 2)
                for g in first_groups[i - 1] if i else []:
                    if g % 2 == 0:
                        place(0, g)
            for g in first_groups[K - 1]:
                if g % 2 == 0:
                    place(0, g)
            place_small(0)
            dve.wait_ge(w1_loaded, 32)
            nc.vector.tensor_tensor(w1_dense[:], w1_first[:], w1_last[:], ALU.add).then_inc(w1_dense_ready, 1)
            dve.wait_ge(weights_loaded, 80)
            for t in range(NT):
                keep_products(t)
                finish_tile(t, t + 1 < NT)
            dve.wait_ge(y_summed, NT)
            nc.vector.tensor_copy(y[:], y_bank[0:1, 0:B]).then_inc(y_ready, 1)

        @block.scalar
        def _(act):
            def widen_and_split(i, q):
                act.wait_ge(table_loaded[q], 16 * (i // 2) + 16)
                if i >= 2:
                    act.wait_ge(small_summed, i - 1)
                nc.scalar.copy(table_hi[:, q, :], table[:, q, :]).then_inc(hi_ready, 1)
                act.wait_ge(ids_wide_ready, i + 1)
                for c in range(TV, TC):
                    nc.scalar.activation(distance[:, c % 2, :], ids_wide[:, bass.ts(i, B)], ACT.Abs,
                                         bias=row_of[:, c:c + 1], scale=-1.0).then_inc(distance_ready, 1)
                    act.wait_ge(distance_ready, (TC - TV) * i + c - TV + 1)
                    nc.scalar.activation(hot[:, q, c, :], distance[:, c % 2, :], ACT.Relu, bias=1.0,
                                         scale=-1.0).then_inc(hot_ready_s, 1)

            def copy_small(i, q):
                act.wait_ge(small_summed, i + 1)
                nc.scalar.copy(small_rows[:, bass.ts(i, B)], g_bank[q][:, 0:B]).then_inc(small_copied, 1)

            def widen(i):
                act.wait_ge(ids_spread, i + 1)
                nc.scalar.copy(ids_wide[:, i * B:i * B + B], spread_bank[i][0:TR, 0:B]).then_inc(ids_wide_ready, 1)

            act.wait_ge(consts_ready, 3)
            nc.scalar.activation(distance[:, 0, 0:TC], row_of[:], ACT.Abs).then_inc(act_warm, 1)
            act.wait_ge(act_warm, 1)
            widen(0)
            widen_and_split(0, 0)
            widen(1)
            widen_and_split(1, 1)
            copy_small(0, 0)
            for i in range(2, K):
                widen(i)

            def place(t, g):
                act.wait_ge(x_turned, NX * t + g + 1)
                copy_group(nc.scalar.copy, g).then_inc(x_ready[1], 1)
                if g == 1 and t > 0:
                    place_small(t)

            def place_small(t):
                act.wait_ge(small_copied, K)
                for n in range(1, K, 2):
                    op = nc.scalar.copy(xt[:, :, small_slot[n]], small_rows[:, n * B + P * t:n * B + P * t + P])
                op.then_inc(small_placed[1], 1)

            def keep_products(t):
                act.wait_ge(x_ready[0], XD * t + dense_group // 2 + 1)
                nc.scalar.copy(dense_t[:], xt[:, :, F - 1]).then_inc(dense_ready, 1)
                for g in range(1, NG, 2):
                    act.wait_ge(g_summed, NG * t + g + 1)
                    nc.scalar.copy(gram[:, GS * g:GS * g + GS, :],
                                   g_bank[1][0:M, 0:GS * M].rearrange("r (s f) -> r s f", f=M),
                                   ).then_inc(g_copied[1], 1)

            def finish_tile(t, between):
                act.wait_ge(zt_turned, t + 1)
                nc.scalar.copy(zt[:], z_bank[0:ZP, 0:ZC * P].rearrange("r (c s) -> r c s", c=ZC)).then_inc(zt_copied, 1)
                if between:
                    place(t + 1, 1)
                act.wait_ge(h1_summed[1], t + 1)
                for c in range(1, C1, 2):
                    op = nc.scalar.activation(h1[:, c, :], h1_out(c), ACT.Relu, bias=b1[:, c:c + 1])
                op.then_inc(h1_ready[1], 1)
                act.wait_ge(h2_summed[1], t + 1)
                nc.scalar.activation(h2[:, 1, :], h2_out[1], ACT.Relu, bias=b2[:, 1:2]).then_inc(h2_ready[1], 1)
                if between:
                    for g in range(3, NX, 2):
                        place(t + 1, g)

            for i in range(2, K + 1):
                if i < K:
                    widen_and_split(i, i % 2)
                copy_small(i - 1, 1 - i % 2)
                for g in first_groups[i - 1]:
                    if g % 2:
                        place(0, g)
            place_small(0)
            act.wait_ge(weights_loaded, 80)
            for t in range(NT):
                keep_products(t)
                finish_tile(t, t + 1 < NT)


def kernel(**inputs):
    import numpy as np
    import concourse.bacc as bacc
    from concourse import mybir as _mybir
    from concourse.bass_utils import run_bass_kernel_spmd

    nc = bacc.Bacc("TRN2", target_bir_lowering=False, num_devices=1)
    arrays, args = {}, {}
    for name, value in inputs.items():
        a = np.ascontiguousarray(value)
        arrays[f"in_{name}"] = a
        args[name] = nc.dram_tensor(f"in_{name}", a.shape, _mybir.dt.from_np(a.dtype), kind="ExternalInput").ap()
    samples = inputs["r_dense_features"].shape[0]
    out = nc.dram_tensor("out_y", (samples, 1), _mybir.dt.float32, kind="ExternalOutput").ap()
    tables = [args[f"tbl_{f}"] for f in range(inputs["ids"].shape[1])]
    dlrm_tower(nc, args["r_dense_features"], args["ids"], tables, args["W_top1"], args["b_top1"],
               args["W_top2"], args["b_top2"], args["W_top3"], out)
    r = run_bass_kernel_spmd(nc, [arrays], core_ids=[0])
    return r.results[0]["out_y"]
```

```python
from contextlib import ExitStack

import concourse.bass as bass
from concourse import mybir

F32 = mybir.dt.float32
F32R = mybir.dt.float32r
F16 = mybir.dt.float16
I32 = mybir.dt.int32
ALU = mybir.AluOpType
ACT = mybir.ActivationFunctionType

P = 128


def dlrm_tower(nc, dense, ids, tables, W_top1, b_top1, W_top2, b_top2, W_top3, out):
    B, D = dense.shape
    T = len(tables)
    F = T + 1
    NT = B // P
    N1, N2 = W_top1.shape[1], W_top2.shape[1]
    C1, C2 = N1 // P, N2 // P
    M = F - 1
    PAIRS = F * (F - 1) // 2
    TB = 4
    LAST = 4
    LOOKUPS = 7
    FREE = 6
    shares = [18, 18, 18, 18, 16, 16, 16, 8]
    NG = len(shares)
    S = 32
    TC = 8

    small = [f for f in range(T) if tables[f].shape[0] <= TC * P and tables[f].shape[0] % TC == 0]
    TR = tables[small[0]].shape[0] // TC
    small = [f for f in small if tables[f].shape[0] == TR * TC][:LOOKUPS]
    K = len(small)
    small_slot = [T - 1 - f for f in small]
    by_vector = [7, 6, 7, 6, 7, 6, 7][:K]
    turned = [r for r in range(F) if r not in small_slot]
    groups = [turned[max(n - 4, LAST):n] for n in range(len(turned), LAST, -4)]
    groups += [turned[1:LAST], turned[0:1]]
    NX = len(groups)
    XD, XA = NX - NX // 2, NX // 2
    dense_group = next(g for g in range(NX) if F - 1 in groups[g])
    assert D == P and F <= S and N1 <= 512 and NT % 2 == 0
    assert sum(shares) == P and NG % 2 == 0 and max(shares) * M <= 512
    assert TR * TC <= 2048 and B <= 512 and NX == 6 and K in (6, 7)

    first_groups = [[], [0], [1], [2], [3], [4, 5]] + [[]] * (K - 6)

    def runs(group):
        found = []
        for k, r in enumerate(group):
            if found and r == found[-1][0] + found[-1][2]:
                found[-1][2] += 1
            else:
                found.append([r, k, 1])
        return found

    def pair_start(f):
        return f * (F - 1) - f * (f - 1) // 2

    H = M // 2
    chunks = [[]]
    sizes = [0]
    for a in range(H):
        count = 2 * F - 2 - a - (H + a)
        if sizes[-1] + count > P:
            chunks.append([])
            sizes.append(0)
        chunks[-1].append((a, H + a, sizes[-1]))
        sizes[-1] += count
    ZC = len(chunks)

    with ExitStack() as ctx:
        def sb(name, shape, dt=F32):
            return ctx.enter_context(nc.sbuf_tensor(name, shape, dt))

        def ps(name):
            return ctx.enter_context(nc.psum_tensor(name, [P, 512], F32))

        def sem(name):
            return ctx.enter_context(nc.semaphore(name))

        ident = sb("ident", [P, P])
        anti = sb("anti", [S + M, M + H])
        orders = sb("orders", [S + M, H, M + S])
        row_of = sb("row_of", [TR, TC])
        ids_sb = sb("ids_sb", [P, NT, T], I32)
        ids_f = sb("ids_f", [P, NT, K])
        ids_t = sb("ids_t", [P, B], F16)
        pick = sb("pick", [P, K, TR], F16)
        ids_wide = sb("ids_wide", [TR, K * B])
        table = sb("table", [TR, TB, TC * D])
        table_hi = sb("table_hi", [TR, 2, TC * D], F32R)
        table_lo = sb("table_lo", [TR, 2, TC * D], F32R)
        distance = sb("distance", [TR, 2, B])
        hot = sb("hot", [TR, 2, TC, B], F32R)
        small_rows = sb("small_rows", [D, K * B])
        rows = sb("rows", [P, 2, F, D])
        xt = sb("xt", [D, P, S])
        gram = sb("gram", [S + M, P, H])
        z = sb("z", [P, ZC, P])
        zt = sb("zt", [P, ZC, P])
        dense_t = sb("dense_t", [D, P])
        h1 = sb("h1", [P, C1, P])
        h2 = sb("h2", [P, 2, C2, P])
        w1_first = sb("w1_first", [D, N1])
        w1_last = sb("w1_last", [D, N1])
        w1_dense = sb("w1_dense", [D, N1])
        w1_pairs = sb("w1_pairs", [P, ZC, N1])
        w2 = sb("w2", [P, C1, N2])
        w3 = sb("w3", [P, C2])
        b1 = sb("b1", [P, C1])
        b2 = sb("b2", [P, C2])
        y = sb("y", [1, P, NT])

        x_bank = [ps("x_bank0"), ps("x_bank1")]
        g_bank = [ps("g_bank0"), ps("g_bank1"), ps("g_bank2")]
        z_bank = ps("z_bank")
        h_bank = [ps("h_bank0"), ps("h_bank1")]
        spread_bank = [x_bank[1], x_bank[0], z_bank, g_bank[0], *h_bank, z_bank]
        small_bank = [g_bank[2 - (K - 1 - i) % 2] for i in range(K)]

        def h1_out(c):
            return h_bank[c % 2][:, c // 2 * P:c // 2 * P + P]

        z_out = [g_bank[2], z_bank, g_bank[0]]
        zt_out = [g_bank[1][:, 0:P], z_bank[:, 0:P], z_bank[:, P:2 * P]]
        h2_out = [h_bank[0][:, 3 * P:4 * P], z_bank[:, 3 * P:4 * P]]

        def y_out(t):
            return (g_bank[2] if t == NT - 2 else h_bank[1])[0:1, 3 * P:4 * P]

        assert C2 == 2 and C1 == 4 and ZC == 3 and NG >= 4

        ids_loaded = sem("ids_loaded")
        all_ids_loaded = sem("all_ids_loaded")
        ids_t_cleared = sem("ids_t_cleared")
        consts_cleared = sem("consts_cleared")
        consts_ready = sem("consts_ready")
        ids_float = sem("ids_float")
        ids_turned = sem("ids_turned")
        ids_t_ready = sem("ids_t_ready")
        ids_spread = sem("ids_spread")
        ids_wide_ready = sem("ids_wide_ready")
        table_loaded = [sem(f"table_loaded{n}") for n in range(TB)]
        act_warm = sem("act_warm")
        hi_ready = sem("hi_ready")
        lo_ready = sem("lo_ready")
        distance_ready = sem("distance_ready")
        hot_ready_v = sem("hot_ready_v")
        hot_ready_s = sem("hot_ready_s")
        small_summed = sem("small_summed")
        small_copied = sem("small_copied")
        gathered = [[sem(f"gathered{p}_{g}") for g in range(NX)] for p in range(2)]
        dense_loaded = [sem("dense_loaded0"), sem("dense_loaded1")]
        w1_loaded = sem("w1_loaded")
        w1_dense_ready = sem("w1_dense_ready")
        weights_loaded = sem("weights_loaded")
        xt_cleared = sem("xt_cleared")
        gram_cleared = sem("gram_cleared")
        orders_ready = sem("orders_ready")
        x_turned = sem("x_turned")
        x_ready = [sem("x_ready_v"), sem("x_ready_s")]
        small_placed = [sem("small_placed_v"), sem("small_placed_s")]
        dense_ready = sem("dense_ready")
        g_summed = sem("g_summed")
        g_copied = [sem("g_copied_v"), sem("g_copied_s")]
        z_turned = sem("z_turned")
        z_copied = sem("z_copied")
        zt_turned = sem("zt_turned")
        zt_copied = sem("zt_copied")
        h1_summed = [sem("h1_summed0"), sem("h1_summed1")]
        h1_ready = [sem("h1_ready_v"), sem("h1_ready_s")]
        h2_summed = [sem("h2_summed0"), sem("h2_summed1")]
        h2_ready = [sem("h2_ready_v"), sem("h2_ready_s")]
        y_summed = sem("y_summed")
        y_ready = sem("y_ready")
        y_stored = sem("y_stored")

        block = ctx.enter_context(nc.Block())

        @block.sync
        def _(sp):
            def load_table(i):
                sp.dma_start(table[:, i % TB, :], tables[small[i]].rearrange("(p c) d -> p (c d)", c=TC),
                             ).then_inc(table_loaded[i % TB], 16)

            def load_dense(t):
                sp.dma_start(rows[:, t % 2, F - 1, :], dense.rearrange("(p t) d -> t p d", p=P)[t],
                             ).then_inc(dense_loaded[t % 2], 16)

            by_tile = ids.rearrange("(p t) f -> p t f", p=P)
            sp.dma_start(ids_sb[:, 0, :], by_tile[:, 0, :]).then_inc(ids_loaded, 16)
            sp.dma_start(ids_sb[:, 1:NT, :], by_tile[:, 1:NT, :]).then_inc(all_ids_loaded, 16)
            load_table(0)
            load_table(1)
            load_dense(0)
            load_dense(1)
            for i in range(2, TB):
                load_table(i)
            sp.dma_start(w1_first[:], W_top1[0:D, :]).then_inc(w1_loaded, 16)
            sp.dma_start(w1_last[:], W_top1[D + PAIRS:D + PAIRS + D, :]).then_inc(w1_loaded, 16)
            for i in range(TB, K):
                sp.wait_ge(hi_ready, i - TB + 1)
                sp.wait_ge(lo_ready, i - TB + 1)
                load_table(i)
            for k in range(ZC):
                for a, b, at in chunks[k]:
                    for f in (a, b):
                        n = F - 1 - f
                        first = D + pair_start(f)
                        sp.dma_start(w1_pairs[at:at + n, k, :], W_top1[first:first + n, :],
                                     ).then_inc(weights_loaded, 16)
                        at += n
            sp.dma_start(w2[:], W_top2.rearrange("(c p) n -> p c n", c=C1)).then_inc(weights_loaded, 16)
            with nc.allow_non_contiguous_dma(reason="columns of a few hundred words, once"):
                sp.dma_start(b1[:], b_top1.rearrange("(c p) -> p c", c=C1)).then_inc(weights_loaded, 16)
                sp.dma_start(b2[:], b_top2.rearrange("(c p) -> p c", c=C2)).then_inc(weights_loaded, 16)
                sp.dma_start(w3[:], W_top3.rearrange("(c p) o -> p (c o)", c=C2)).then_inc(weights_loaded, 16)
            for t in range(2, NT):
                sp.wait_ge(x_turned, NX * (t - 1))
                load_dense(t)
            sp.wait_ge(y_ready, NT)
            sp.dma_start(out.rearrange("n o -> o n"), y[:].rearrange("o p t -> o (p t)")).then_inc(y_stored, 16)
            sp.wait_ge(y_stored, 16)

        @block.gpsimd
        def _(pool):
            nc.gpsimd.memset(ident[:], 0.0).then_inc(consts_cleared, 1)
            nc.gpsimd.memset(anti[:], 0.0).then_inc(consts_cleared, 1)
            pool.wait_ge(consts_cleared, 2)
            nc.gpsimd.affine_select(out=ident[:], in_=ident[:], compare_op=ALU.not_equal, fill=1.0, base=0,
                                    pattern=[[-1, P]], channel_multiplier=1).then_inc(consts_ready, 1)
            for last, at, n in ((S + M - 1, 0, M), (H - 1, M, H)):
                nc.gpsimd.affine_select(out=anti[:, at:at + n], in_=anti[:, at:at + n], compare_op=ALU.not_equal,
                                        fill=1.0, base=-last, pattern=[[1, n]], channel_multiplier=1,
                                        ).then_inc(consts_ready, 1)
            nc.gpsimd.iota(row_of[:], pattern=[[1, TC]], base=0, channel_multiplier=TC,
                           allow_small_or_imprecise_dtypes=True).then_inc(consts_ready, 1)
            nc.gpsimd.memset(gram[0:S, 0:P // 2, :], 0.0).then_inc(gram_cleared, 1)
            pool.wait_ge(ids_loaded, 16)
            for t in range(NT):
                if t == 1:
                    pool.wait_ge(all_ids_loaded, 16)
                if t >= 2:
                    pool.wait_ge(x_turned, NX * (t - 1))
                for g in range(NX):
                    for r in groups[g]:
                        if r < T:
                            pool.indirect_dma_start(
                                rows[:, t % 2, r, :], None, tables[T - 1 - r],
                                bass.IndirectOffsetOnAxis(ids_sb[:, t, T - 1 - r:T - r], 0),
                            ).then_inc(gathered[t % 2][g], 16)

        @block.tensor
        def _(pe):
            def spread_ids():
                pe.wait_ge(consts_ready, 4)
                pe.wait_ge(ids_float, 1)
                for t in range(NT):
                    mm = pe.transpose(x_bank[0][0:K, t * P:t * P + P], ids_f[:, t, :], ident[:])
                mm.then_inc(ids_turned, 1)
                pe.wait_ge(ids_t_ready, 1)
                for i in range(min(K, FREE)):
                    spread(i)

            def spread(i):
                pe.matmul(spread_bank[i][0:TR, 0:B], pick[:, i, :], ids_t[:], start=True,
                          stop=True).then_inc(ids_spread, 1)

            def look_up(i, q):
                pe.wait_ge(hi_ready, i + 1)
                if i >= 2:
                    pe.wait_ge(small_copied, i - 1)
                for c in range(TC):
                    if c < by_vector[i]:
                        pe.wait_ge(hot_ready_v, sum(by_vector[:i]) + c + 1)
                    else:
                        pe.wait_ge(hot_ready_s, TC * i - sum(by_vector[:i + 1]) + c + 1)
                    pe.matmul(small_bank[i][:, 0:B], table_hi[:, q, c * D:c * D + D], hot[:, q, c, :],
                              start=(c == 0), stop=False)
                pe.wait_ge(lo_ready, i + 1)
                for c in range(TC):
                    mm = pe.matmul(small_bank[i][:, 0:B], table_lo[:, q, c * D:c * D + D], hot[:, q, c, :],
                                   start=False, stop=(c == TC - 1))
                mm.then_inc(small_summed, 1)

            def turn_group(p, i, g):
                t = 2 * i + p
                n = sum(r < T for r in groups[g])
                pe.wait_ge(gathered[p][g], 16 * n * i + 16 * n)
                if g == dense_group:
                    pe.wait_ge(dense_loaded[p], 16 * i + 16)
                if g >= 2:
                    pe.wait_ge(x_ready[g % 2], (XD, XA)[g % 2] * t + g // 2)
                for k, r in enumerate(groups[g]):
                    mm = pe.transpose(x_bank[g % 2][:, k * P:k * P + P], rows[:, p, r, :], ident[:])
                mm.then_inc(x_turned, 1)

            def interact(t):
                if t == 0:
                    pe.wait_ge(xt_cleared, 1)
                    pe.wait_ge(x_ready[1], XA)
                    pe.wait_ge(x_ready[0], XD)
                pe.wait_ge(small_placed[0], t + 1)
                pe.wait_ge(small_placed[1], t + 1)
                if t > 0:
                    pe.wait_ge(x_ready[0], XD * t + XD)
                    pe.wait_ge(x_ready[1], XA * t + XA)
                for g in range(NG):
                    if t == 0 and g == 2:
                        pe.wait_ge(small_copied, K)
                    if g >= 3:
                        pe.wait_ge(g_copied[(g - 3) % 2], NG // 2 * t + (g - 3) // 2 + 1)
                    for k in range(0, shares[g], 2):
                        s = sum(shares[:g]) + k
                        two = xt[:, s:s + 2, :]
                        mm = pe.matmul(g_bank[g % 3][0:S + M, k * M:(k + 2) * M],
                                       two.rearrange("d s r -> d (s r)")[:, 0:S + M], two[:, :, 1:F],
                                       start=True, stop=True)
                    mm.then_inc(g_summed, 1)
                    if g == 1 and 0 < t < NT - 1:
                        layer3(t - 1)

            def layer1_dense(t, cs):
                pe.wait_ge(dense_ready, t + 1)
                if 0 < t < NT - 1:
                    pe.wait_ge(y_ready, t)
                for c in cs:
                    pe.matmul(h1_out(c), w1_dense[:, c * P:c * P + P], dense_t[:], start=(c < 2), stop=False,
                              skip_group_check=True)

            def pairs(t):
                pe.wait_ge(g_copied[0], NG // 2 * t + NG // 2)
                pe.wait_ge(g_copied[1], NG // 2 * t + NG // 2)
                for k in range(ZC):
                    for a, b, at in chunks[k]:
                        n = F - 1 - a
                        mm = pe.transpose(z_out[k][:, at:at + n + S], gram[0:S + n, :, H - 1 - a],
                                          orders[0:S + n, a, 0:S + n])
                    mm.then_inc(z_turned, 1)

            def turn_pairs(t, k):
                pe.wait_ge(z_copied, ZC * t + k + 1)
                pe.transpose(zt_out[k][0:sizes[k], :], z[:, k, 0:sizes[k]], ident[:]).then_inc(zt_turned, 1)

            def layer1_pairs(t, ks, bank):
                for c in range(bank, C1, 2):
                    for k in ks:
                        n = sizes[k]
                        mm = pe.matmul(h1_out(c), w1_pairs[0:n, k, c * P:c * P + P], zt[0:n, k, :],
                                       start=False, stop=(k == ZC - 1), skip_group_check=True)
                return mm

            def layer2(t, half):
                pe.wait_ge(h1_ready[half], t + 1)
                for c in range(C2):
                    for k in range(half, C1, 2):
                        mm = pe.matmul(h2_out[c], w2[:, k, c * P:c * P + P], h1[:, k, :],
                                       start=(k == 0), stop=(k == C1 - 1))
                    if half == 1:
                        mm.then_inc(h2_summed[c], 1)

            def layer3(t):
                for c in range(C2):
                    pe.wait_ge(h2_ready[c], t + 1)
                    mm = pe.matmul(y_out(t), w3[:, c:c + 1], h2[:, t % 2, c, :], start=(c == 0), stop=(c == C2 - 1))
                mm.then_inc(y_summed, 1)

            def finish_tile(t):
                last = t + 1 == NT

                def between(*gs):
                    if not last:
                        for g in gs:
                            turn_group((t + 1) % 2, (t + 1) // 2, g)

                between(0, 1)
                if last:
                    layer1_dense(t, range(C1 - 1))
                pairs(t)
                turn_pairs(t, 0)
                turn_pairs(t, 1)
                layer1_dense(t, [C1 - 1] if last else range(C1))
                turn_pairs(t, 2)
                between(2)
                pe.wait_ge(zt_copied, 2 * t + 1)
                layer1_pairs(t, [0], 0)
                layer1_pairs(t, [0], 1)
                between(3)
                pe.wait_ge(zt_copied, 2 * t + 2)
                for bank in range(2):
                    layer1_pairs(t, [1, 2], bank).then_inc(h1_summed[bank], 1)
                if t < NT - 2:
                    between(4)
                    layer2(t, 0)
                    between(5)
                    layer2(t, 1)
                else:
                    layer2(t, 0)
                    between(4)
                    layer2(t, 1)
                    between(5)

            spread_ids()
            for i in range(K):
                look_up(i, i % 2)
                if i == 1:
                    pe.wait_ge(ids_wide_ready, 2)
                if i == 3 and K > FREE:
                    pe.wait_ge(ids_wide_ready, 3)
                    spread(FREE)
                for g in first_groups[i]:
                    turn_group(0, 0, g)
            pe.wait_ge(ids_wide_ready, K)
            pe.wait_ge(small_copied, K - 1)
            for t in range(NT):
                interact(t)
                if t == 0:
                    pe.wait_ge(orders_ready, 2)
                    pe.wait_ge(w1_dense_ready, 1)
                    pe.wait_ge(weights_loaded, 16 * (M + 4))
                finish_tile(t)
            layer3(NT - 2)
            layer3(NT - 1)

        def copy_group(eng_copy, g):
            for r, k, n in runs(groups[g]):
                op = eng_copy(
                    xt[:, :, r:r + n].rearrange("d s r -> d r s"),
                    x_bank[g % 2][:, k * P:(k + n) * P].rearrange("d (r s) -> d r s", r=n),
                )
            return op

        def products(g):
            s = sum(shares[:g])
            two = g_bank[g % 3][:, 0:shares[g] * M].rearrange("r (k s f) -> r k s f", s=2, f=M)
            there = gram[:, s:s + shares[g], :].rearrange("r (k s) f -> r k s f", s=2)
            return [(there[S * half:S * half + M, :, odd, :], two[S * odd:S * odd + M, :, odd, H * half:H * half + H])
                    for half in range(2) for odd in range(2)]

        @block.vector
        def _(dve):
            nc.vector.memset(xt[:, :, F:S], 0.0).then_inc(xt_cleared, 1)
            nc.vector.memset(ids_t[:], 0.0).then_inc(ids_t_cleared, 1)
            dve.wait_ge(consts_ready, 4)
            for n in range(K):
                nc.vector.tensor_copy(pick[:, n, :], ident[:, n:n + 1].to_broadcast([P, TR]))
            dve.wait_ge(ids_loaded, 16)
            dve.wait_ge(all_ids_loaded, 16)
            for f, n, m in runs(small):
                op = nc.vector.tensor_copy(ids_f[:, :, n:n + m], ids_sb[:, :, f:f + m])
            op.then_inc(ids_float, 1)
            dve.wait_ge(ids_turned, 1)
            dve.wait_ge(ids_t_cleared, 1)
            nc.vector.tensor_copy(ids_t[0:K, :], x_bank[0][0:K, 0:B]).then_inc(ids_t_ready, 1)

            def split_and_mark(i, q):
                if i >= 2:
                    dve.wait_ge(small_summed, i - 1)
                dve.wait_ge(ids_wide_ready, i + 1)
                for c in range(by_vector[i]):
                    nc.vector.tensor_scalar(hot[:, q, c, :], ids_wide[:, bass.ts(i, B)], row_of[:, c:c + 1], None,
                                            ALU.is_equal).then_inc(hot_ready_v, 1)
                dve.wait_ge(hi_ready, i + 1)
                nc.vector.tensor_tensor(table_lo[:, q, :], table[:, i % TB, :], table_hi[:, q, :].bitcast(F32),
                                        ALU.subtract).then_inc(lo_ready, 1)

            def place(t, g):
                dve.wait_ge(x_turned, NX * t + g + 1)
                copy_group(nc.vector.tensor_copy, g).then_inc(x_ready[0], 1)

            def place_small(t):
                dve.wait_ge(small_copied, K if t else K - 1)
                for n in range(0, K, 2) if t else range(K - 1):
                    op = nc.vector.tensor_copy(xt[:, :, small_slot[n]], small_rows[:, n * B + P * t:n * B + P * t + P])
                op.then_inc(small_placed[0], 1)

            def keep_products(t):
                for g in range(0, NG, 2):
                    dve.wait_ge(g_summed, NG * t + g + 1)
                    for there, here in products(g):
                        op = nc.vector.tensor_copy(there, here)
                    op.then_inc(g_copied[0], 1)
                    if t == 0 and g == 0:
                        dve.wait_ge(w1_loaded, 32)
                        nc.vector.tensor_tensor(w1_dense[:], w1_first[:], w1_last[:], ALU.add,
                                                ).then_inc(w1_dense_ready, 1)
                    if g == 2 and 0 < t < NT - 1:
                        keep_y(t - 1)

            def finish_tile(t):
                def between(g):
                    if t + 1 < NT:
                        place(t + 1, g)

                between(0)
                for k in range(ZC):
                    dve.wait_ge(z_turned, ZC * t + k + 1)
                    nc.vector.tensor_copy(z[:, k, 0:sizes[k]], z_out[k][:, 0:sizes[k]]).then_inc(z_copied, 1)
                if t + 1 < NT:
                    place_small(t + 1)
                between(2)
                dve.wait_ge(h1_summed[0], t + 1)
                for c in range(0, C1, 2):
                    op = nc.vector.tensor_scalar(h1[:, c, :], h1_out(c), b1[:, c:c + 1], 0.0, ALU.add, ALU.max)
                op.then_inc(h1_ready[0], 1)
                between(4)
                dve.wait_ge(h2_summed[0], t + 1)
                nc.vector.tensor_scalar(h2[:, t % 2, 0, :], h2_out[0], b2[:, 0:1], 0.0, ALU.add,
                                        ALU.max).then_inc(h2_ready[0], 1)

            def keep_y(t):
                dve.wait_ge(y_summed, t + 1)
                nc.vector.tensor_copy(y[:, :, t], y_out(t)).then_inc(y_ready, 1)

            for i in range(K):
                split_and_mark(i, i % 2)
                for g in first_groups[i - 1] if i else []:
                    if g % 2 == 0:
                        place(0, g)
            for g in first_groups[K - 1]:
                if g % 2 == 0:
                    place(0, g)
            place_small(0)
            nc.vector.memset(gram[0:S, P // 2:, :], 0.0).then_inc(gram_cleared, 1)
            for a in range(H):
                n, m = F - 1 - a, F - 1 - (H + a)
                nc.vector.tensor_copy(orders[:, a, 0:n], anti[:, M - n:M])
                op = nc.vector.tensor_copy(orders[:, a, n:n + m], anti[:, M + H - m:M + H])
            op.then_inc(orders_ready, 1)
            dve.wait_ge(weights_loaded, 16 * (M + 4))
            dve.wait_ge(gram_cleared, 2)
            for t in range(NT):
                keep_products(t)
                finish_tile(t)
            keep_y(NT - 2)
            keep_y(NT - 1)

        @block.scalar
        def _(act):
            def split_and_mark(i, q):
                act.wait_ge(table_loaded[i % TB], 16 * (i // TB) + 16)
                if i >= 2:
                    act.wait_ge(small_summed, i - 1)
                nc.scalar.copy(table_hi[:, q, :], table[:, i % TB, :]).then_inc(hi_ready, 1)
                act.wait_ge(ids_wide_ready, i + 1)
                for c in range(by_vector[i], TC):
                    nc.scalar.activation(distance[:, c % 2, :], ids_wide[:, bass.ts(i, B)], ACT.Abs,
                                         bias=row_of[:, c:c + 1], scale=-1.0).then_inc(distance_ready, 1)
                for c in range(by_vector[i], TC):
                    act.wait_ge(distance_ready, TC * i - sum(by_vector[:i + 1]) + c + 1)
                    nc.scalar.activation(hot[:, q, c, :], distance[:, c % 2, :], ACT.Relu, bias=1.0,
                                         scale=-1.0).then_inc(hot_ready_s, 1)

            def copy_small(i):
                act.wait_ge(small_summed, i + 1)
                if i == K - 1:
                    nc.scalar.copy(xt[:, 0:P, small_slot[i]], small_bank[i][:, 0:P]).then_inc(small_placed[1], 1)
                nc.scalar.copy(small_rows[:, bass.ts(i, B)], small_bank[i][:, 0:B]).then_inc(small_copied, 1)

            def widen(i):
                act.wait_ge(ids_spread, i + 1)
                nc.scalar.copy(ids_wide[:, i * B:i * B + B], spread_bank[i][0:TR, 0:B]).then_inc(ids_wide_ready, 1)

            act.wait_ge(consts_ready, 4)
            nc.scalar.activation(distance[:, 0, 0:TC], row_of[:], ACT.Abs).then_inc(act_warm, 1)
            act.wait_ge(act_warm, 1)

            def place(t, g):
                act.wait_ge(x_turned, NX * t + g + 1)
                copy_group(nc.scalar.copy, g).then_inc(x_ready[1], 1)
                if g == 1 and t > 0:
                    place_small(t)

            def place_small(t):
                act.wait_ge(small_copied, K)
                for n in range(1, K, 2):
                    op = nc.scalar.copy(xt[:, :, small_slot[n]], small_rows[:, n * B + P * t:n * B + P * t + P])
                op.then_inc(small_placed[1], 1)

            def keep_products(t):
                act.wait_ge(x_ready[dense_group % 2], NX // 2 * t + dense_group // 2 + 1)
                nc.scalar.copy(dense_t[:], xt[:, :, F - 1]).then_inc(dense_ready, 1)
                for g in range(1, NG, 2):
                    act.wait_ge(g_summed, NG * t + g + 1)
                    for there, here in products(g):
                        op = nc.scalar.copy(there, here)
                    op.then_inc(g_copied[1], 1)

            def finish_tile(t):
                def between(g):
                    if t + 1 < NT:
                        place(t + 1, g)

                between(1)
                act.wait_ge(zt_turned, ZC * t + 1)
                nc.scalar.copy(zt[0:sizes[0], 0, :], zt_out[0][0:sizes[0], :]).then_inc(zt_copied, 1)
                for k in range(1, ZC):
                    act.wait_ge(zt_turned, ZC * t + ZC)
                    op = nc.scalar.copy(zt[0:sizes[k], k, :], zt_out[k][0:sizes[k], :])
                op.then_inc(zt_copied, 1)
                between(3)
                act.wait_ge(h1_summed[1], t + 1)
                for c in range(1, C1, 2):
                    op = nc.scalar.activation(h1[:, c, :], h1_out(c), ACT.Relu, bias=b1[:, c:c + 1])
                op.then_inc(h1_ready[1], 1)
                between(5)
                act.wait_ge(h2_summed[1], t + 1)
                nc.scalar.activation(h2[:, t % 2, 1, :], h2_out[1], ACT.Relu, bias=b2[:, 1:2]).then_inc(h2_ready[1], 1)

            for i in range(K + 1):
                if i < K:
                    widen(i)
                    split_and_mark(i, i % 2)
                if i == K:
                    for a in range(H):
                        n, m = F - 1 - a, F - 1 - (H + a)
                        op = nc.scalar.copy(orders[:, a, n + m:n + S], ident[0:S + M, m:S])
                    op.then_inc(orders_ready, 1)
                if i > 0:
                    copy_small(i - 1)
                    for g in first_groups[i - 1]:
                        if g % 2:
                            place(0, g)
            act.wait_ge(weights_loaded, 16 * (M + 4))
            act.wait_ge(gram_cleared, 2)
            for t in range(NT):
                keep_products(t)
                finish_tile(t)


def kernel(**inputs):
    import numpy as np
    import concourse.bacc as bacc
    from concourse import mybir as _mybir
    from concourse.bass_utils import run_bass_kernel_spmd

    nc = bacc.Bacc("TRN2", target_bir_lowering=False, num_devices=1)
    arrays, args = {}, {}
    for name, value in inputs.items():
        a = np.ascontiguousarray(value)
        arrays[f"in_{name}"] = a
        args[name] = nc.dram_tensor(f"in_{name}", a.shape, _mybir.dt.from_np(a.dtype), kind="ExternalInput").ap()
    samples = inputs["r_dense_features"].shape[0]
    out = nc.dram_tensor("out_y", (samples, 1), _mybir.dt.float32, kind="ExternalOutput").ap()
    tables = [args[f"tbl_{f}"] for f in range(inputs["ids"].shape[1])]
    dlrm_tower(nc, args["r_dense_features"], args["ids"], tables, args["W_top1"], args["b_top1"],
               args["W_top2"], args["b_top2"], args["W_top3"], out)
    r = run_bass_kernel_spmd(nc, [arrays], core_ids=[0])
    return r.results[0]["out_y"]
```
